# Optimizing a Trainium2 kernel written in Bass

```python
import numpy as np
import jax
import jax.numpy as jnp

def _softmax(x, axis=-1):
    return jax.nn.softmax(x, axis=axis)

def _gelu(x):
    return jax.nn.gelu(x, approximate=True)

def _silu(x):
    return jax.nn.silu(x)

def _sigmoid(x):
    return jax.nn.sigmoid(x)

def _layernorm(x, axis=-1, eps=1e-05):
    m = jnp.mean(x, axis=axis, keepdims=True)
    v = jnp.var(x, axis=axis, keepdims=True)
    return (x - m) / jnp.sqrt(v + eps)

def _scatter_add(tgt, idx, src, axis=0):
    return tgt.at[idx].add(src)

def _segment_sum(src, seg, n):
    return jax.ops.segment_sum(src, seg, n)
kernel_name = 'mk_adj_preln_d1_adj_r2_f75024'

def setup_inputs(seed: int=0):
    np.random.seed(seed)
    _w = jnp.asarray

    def _rec_inputs():
        import jax
        import jax.numpy as jnp
        _gk = jax.random.key(seed)
        x = -0.001003 + 1 * jax.random.normal(jax.random.fold_in(_gk, 1), (6144, 128), jnp.float32)
        _w = (1.0 + jnp.arange(6144, dtype=jnp.float32)) ** (-0.5)
        _w = _w / _w.mean()
        _pij = jnp.clip(0.00260417 * _w[:, None] * _w[None, :], 0.0, 1.0)
        _a = jax.random.uniform(jax.random.fold_in(_gk, 2), (6144, 6144)) < _pij
        adj = _a.astype(jnp.int32)
        return (x, adj)
    x, adj = _rec_inputs()

    def _L0_gnn_setup():
        import jax, jax.numpy as jnp
        import numpy as np
        M = 6144
        N = 6144
        D = 128
        TEMPERATURE = 0.07
        NEG_PAD = jnp.float32(-2 ** 32 + 1)
        key = jax.random.key(seed)
        k1, k2, k3, k4 = jax.random.split(key, 4)
        xx_anchor = jax.random.normal(k1, (M, D), dtype=jnp.float32)
        inp = jax.random.normal(k2, (N, D), dtype=jnp.float32)
        adj = (jax.random.uniform(k3, (M, N)) < 0.002).astype(jnp.int32)
        limit = jnp.sqrt(6.0 / (D + D)).astype(jnp.float32)
        weight = jax.random.uniform(k4, (D, D), minval=-limit, maxval=limit, dtype=jnp.float32)
        return {'xx_anchor': xx_anchor, 'input': inp, 'adj': adj, 'weight': weight}
    _L0_gnn_all = _L0_gnn_setup()
    _L0_gnn_in = {k: v for k, v in _L0_gnn_all.items() if k in ('input', 'weight')}
    del _L0_gnn_all
    return {'x': x, 'adj': adj, 'L0_gnn_input': _L0_gnn_in['input'], 'L0_gnn_weight': _L0_gnn_in['weight']}

def reference(x, adj, L0_gnn_input, L0_gnn_weight):
    import jax
    import jax.numpy as jnp

    def _L0_gnn_ref(xx_anchor, input, adj, weight):
        import jax, jax.numpy as jnp
        import numpy as np
        M = 6144
        N = 6144
        D = 128
        TEMPERATURE = 0.07
        NEG_PAD = jnp.float32(-2 ** 32 + 1)
        anchor_adj = jnp.einsum('md,de,ne->mn', xx_anchor, weight, input)
        scores = jnp.where(adj > 0, anchor_adj, NEG_PAD)
        atten = jax.nn.softmax(scores / TEMPERATURE, axis=1)
        return atten @ input
    h = jnp.maximum(_layernorm(x, axis=-1), 0.0)
    x = x + _L0_gnn_ref(h, L0_gnn_input, adj, L0_gnn_weight)
    return x

_drawn_inputs = setup_inputs


def setup_inputs(seed=0):
    import zlib

    import numpy as np

    out = dict(_drawn_inputs(seed))
    spreads = {}
    factors = {}
    for name, (base, spread) in spreads.items():
        noise = np.random.default_rng([zlib.crc32(name.encode()), seed]).standard_normal(out[name].shape)
        drawn = base * np.exp(spread * noise) if base else spread * noise
        out[name] = jnp.asarray(drawn.astype(out[name].dtype))
    for name, factor in factors.items():
        out[name] = (out[name] * factor).astype(out[name].dtype)
    return out
```

```python
from contextlib import ExitStack

import concourse.bass as bass
from concourse import mybir

ALU = mybir.AluOpType
ACT = mybir.ActivationFunctionType
AX = mybir.AxisListType
F32 = mybir.dt.float32
F16 = mybir.dt.float16
BF16 = mybir.dt.bfloat16
I32 = mybir.dt.int32

P = 128
TEMPERATURE = 0.07000000029802322
EPS = 1e-5
BIG = 2.0 ** 100
LIFT = 9.0

CHUNK = 512
PAIR = 2 * CHUNK
THIRD = 2048
TILES = 2
ROWS = TILES * P
ADJ_RING, BIAS_RING, PART_RING = 4, 2, 4

LAG = 28
WEIGH = 2
EXP_AT = 15


def adjacency_attention(nc, x, adj, inp, weight, out):
    M, D = x.shape
    N = inp.shape[0]
    assert D == P and adj.shape == (M, N)
    CHUNKS = N // CHUNK
    PAIRS = N // PAIR
    THIRDS = N // THIRD
    BLOCKS = N // P
    GROUP_STEPS = TILES * CHUNKS
    BODY = 2 * GROUP_STEPS
    SLOTS = BODY // CHUNKS
    STEPS = M // P * CHUNKS
    GROUPS = M // ROWS
    BODIES = STEPS // BODY
    assert STEPS % BODY == 0 and 2 * GROUP_STEPS == BLOCKS
    TAIL = LAG + WEIGH + 4
    BODY_THIRDS = SLOTS * THIRDS

    inp_view = inp.rearrange("(b p) d -> p b d", p=P)
    x_view = x.rearrange("(g t p) d -> p g t d", p=P, t=TILES)
    out_view = out.rearrange("(g t p) d -> p g t d", p=P, t=TILES)
    adj_view = adj.rearrange("(t p) n -> p t n", p=P)

    with ExitStack() as ctx:
        def sb(name, shape, dt):
            return ctx.enter_context(nc.sbuf_tensor(name, shape, dt))

        def psum(name, shape):
            return ctx.enter_context(nc.psum_tensor(name, shape, F32))

        def sem(name):
            return ctx.enter_context(nc.semaphore(name))

        probs = sb("probs", [P, SLOTS, N], F32)
        kT = [sb("kT_hi", [P, N], F16), sb("kT_lo", [P, N], F16)]
        val = [sb("val_hi", [P, BLOCKS, D], F16), sb("val_lo", [P, BLOCKS, D], F16)]
        adj_sb = sb("adj_sb", [P, ADJ_RING, THIRD], I32)
        bias = sb("bias", [P, BIAS_RING, THIRD], BF16)
        part_hi = sb("part_hi", [P, PART_RING, CHUNK], F16)
        part_lo = sb("part_lo", [P, PART_RING, CHUNK], F16)
        qT = [sb("qT_hi", [P, 2, ROWS], F16), sb("qT_lo", [P, 2, ROWS], F16)]
        ident = sb("ident", [P, P], F32)
        w_sb = sb("w_sb", [P, D], F32)
        x_norm = sb("x_norm", [P, 2, TILES, D], F32)
        x_res = sb("x_res", [P, 2, TILES, D], F32)
        stats = sb("stats", [P, TILES, 6], F32)
        moments = sb("moments", [P, TILES, 2], F32)
        var_eps = sb("var_eps", [P, TILES], F32)
        rstd = sb("rstd", [P, TILES], F32)
        minus_half = sb("minus_half", [P, TILES], F32)
        hT = sb("hT", [P, ROWS], F32)
        part_max = sb("part_max", [P, 2, PAIRS], F32)
        row_max = sb("row_max", [P, SLOTS], F32)
        exp_bias = sb("exp_bias", [P, SLOTS], F32)
        part_sum = sb("part_sum", [P, SLOTS, PAIRS], F32)
        row_sum = sb("row_sum", [P, TILES], F32)
        inv_sum = sb("inv_sum", [P, TILES], F32)
        accT_sb = sb("accT_sb", [P, ROWS], F32)
        result = sb("result", [P, 2, TILES, D], F32)
        inp_sb = probs[:, SLOTS - 1, :].rearrange("p (b d) -> p b d", d=D)

        ps_scores = psum("ps_scores", [P, 2, PAIR])
        ps_turn = psum("ps_turn", [P, 2, CHUNK])
        ps_acc = psum("ps_acc", [P, CHUNK])
        ps_misc = psum("ps_misc", [P, CHUNK])

        inp_landed = [sem(f"inp_landed{c}") for c in range(4)]
        w_landed = sem("w_landed")
        x_landed = [sem(f"x_landed{c}") for c in range(2)]
        res_landed = [sem(f"res_landed{c}") for c in range(2)]
        adj_landed = [sem(f"adj_landed{c}") for c in range(ADJ_RING)]
        stored = [sem(f"stored{c}") for c in range(2)]
        wait_over = [sem("wait_over_vector"), sem("wait_over_gpsimd")]
        ident_blank = sem("ident_blank")
        ident_ready = sem("ident_ready")
        half_ready = sem("half_ready")
        bias_ready = sem("bias_ready")
        var_ready = sem("var_ready")
        rstd_ready = sem("rstd_ready")
        stats_ready = sem("stats_ready")
        moments_ready = sem("moments_ready")
        norm_ready = sem("norm_ready")
        hT_ready = sem("hT_ready")
        hT_copied = sem("hT_copied")
        qT_ready = sem("qT_ready")
        q_hi_ready = sem("q_hi_ready")
        q_lo_ready = sem("q_lo_ready")
        keys_turned = sem("keys_turned")
        k_hi_ready = sem("k_hi_ready")
        k_lo_ready = sem("k_lo_ready")
        v_hi_ready = sem("v_hi_ready")
        v_lo_ready = sem("v_lo_ready")
        scores_ready = sem("scores_ready")
        masked = sem("masked")
        max_found = sem("max_found")
        exp_bias_ready = sem("exp_bias_ready")
        probs_ready = sem("probs_ready")
        turned = sem("turned")
        hi_ready = sem("hi_ready")
        lo_ready = sem("lo_ready")
        weighed = sem("weighed")
        acc_copied = sem("acc_copied")
        acc_turned = sem("acc_turned")
        sum_ready = sem("sum_ready")
        inv_ready = sem("inv_ready")
        result_ready = sem("result_ready")

        def live(i, k, per_body, last):
            return not isinstance(i, int) or 0 <= per_body * i + k < last

        def wait(eng, semaphore, i, per_body, count):
            if not isinstance(i, int):
                eng.wait_ge(semaphore, i * per_body + count)
            elif per_body * i + count > 0:
                eng.wait_ge(semaphore, per_body * i + count)

        def detach(eng):
            eng.sem_inc(wait_over[eng is nc.gpsimd], 1)

        def run(eng, step):
            for s in range(BODY):
                step(0, s)
            with eng.Fori(1, BODIES - 1) as i:
                for s in range(BODY):
                    step(i, s)
            for s in range(BODY + TAIL):
                step(BODIES - 1, s)

        block = ctx.enter_context(nc.Block())

        @block.sync
        def _(sp):
            def load_adj(i, r):
                wait(sp, bias_ready, i, BODY_THIRDS, r - ADJ_RING + 1)
                tile = i * SLOTS + r // THIRDS
                c = r % THIRDS * THIRD
                sp.dma_start(adj_sb[:, r % ADJ_RING, :],
                             adj_view[:, tile, c:c + THIRD] if isinstance(i, int) else
                             adj_view[:, bass.ds(tile, 1), c:c + THIRD].rearrange("p o n -> p (o n)"))\
                    .then_inc(adj_landed[r % ADJ_RING], 16)

            def group_of(view, i, g):
                if isinstance(i, int):
                    return view[:, 2 * i + g]
                return view[:, bass.ds(i * 2 + g, 1)].rearrange("p o t d -> p (o t) d")

            def load_x(i, g):
                wait(sp, hT_ready, i, 2, g - 1)
                sp.dma_start(x_norm[:, g % 2], group_of(x_view, i, g)).then_inc(x_landed[g % 2], 16)

            def load_res(i, g):
                wait(sp, result_ready, i, 2, g - 1)
                sp.dma_start(x_res[:, g % 2], group_of(x_view, i, g)).then_inc(res_landed[g % 2], 16)

            def store(i, g):
                wait(sp, result_ready, i, 2, g + 1)
                sp.dma_start(group_of(out_view, i, g), result[:, g % 2]).then_inc(stored[g % 2], 16)

            load_x(0, 0)
            sp.dma_start(w_sb[:], weight).then_inc(w_landed, 16)
            part = BLOCKS // 4
            for c in range(4):
                sp.dma_start(inp_sb[:, c * part:(c + 1) * part, :], inp_view[:, c * part:(c + 1) * part, :])\
                    .then_inc(inp_landed[c], 16)

            def step(i, s):
                if s % 4 == 0 and live(i, s // 4, BODY_THIRDS, STEPS // 4):
                    load_adj(i, s // 4)
                g = s // GROUP_STEPS
                if s % GROUP_STEPS == 4 and live(i, g + 1, 2, GROUPS):
                    load_x(i, g + 1)
                if s % GROUP_STEPS == 20 and live(i, g - 1, 2, GROUPS):
                    load_res(i, g - 1)
                if s % GROUP_STEPS == 9 and live(i, g - 2, 2, GROUPS):
                    store(i, g - 2)

            run(sp, step)
            for c in range(2):
                sp.wait_ge(stored[c], 16 * GROUPS // 2)

        @block.gpsimd
        def _(pool):
            pool.memset(minus_half[:], -0.5).then_inc(half_ready, 1)
            pool.memset(ident[:], 0.0).then_inc(ident_blank, 1)
            pool.wait_ge(ident_blank, 1)
            pool.affine_select(out=ident[:], in_=ident[:], compare_op=ALU.not_equal, fill=1.0, base=0,
                               pattern=[[-1, P]], channel_multiplier=1).then_inc(ident_ready, 1)
            pool.wait_ge(half_ready, 1)

            def invert_deviation(i, g):
                wait(pool, moments_ready, i, 2, g + 1)
                wait(pool, norm_ready, i, 2, g)
                detach(pool)
                pool.tensor_scalar(var_eps[:], moments[:, :, 1], EPS, None, ALU.add).then_inc(var_ready, 1)
                wait(pool, var_ready, i, 2, g + 1)
                pool.tensor_tensor(rstd[:], var_eps[:], minus_half[:], ALU.pow).then_inc(rstd_ready, 1)

            invert_deviation(0, 0)

            def make_bias(i, r):
                a = adj_sb[:, r % ADJ_RING, :]
                wait(pool, adj_landed[r % ADJ_RING], i, 16 * BODY_THIRDS // ADJ_RING, 16 * (r // ADJ_RING + 1))
                wait(pool, masked, i, BODY_THIRDS * 2, 2 * (r - BIAS_RING) + 2)
                detach(pool)
                pool.tensor_scalar(bias[:, r % BIAS_RING, :], a, 0.0, -BIG, ALU.is_le, ALU.mult)\
                    .then_inc(bias_ready, 1)

            def step(i, s):
                if s % 4 == 0 and live(i, s // 4, BODY_THIRDS, STEPS // 4):
                    make_bias(i, s // 4)
                g = s // GROUP_STEPS
                if s % GROUP_STEPS == 8 and live(i, g + 1, 2, GROUPS):
                    invert_deviation(i, g + 1)

            run(pool, step)

        @block.tensor
        def _(pe):
            def turn_keys(c):
                if c >= 2:
                    pe.wait_ge(k_lo_ready, c - 1)
                for b in range(4):
                    mm = pe.transpose(ps_turn[:, c % 2, b * P:(b + 1) * P], inp_sb[:, 4 * c + b, :], ident[:])
                mm.then_inc(keys_turned, 1)

            def turn_h(i, g):
                wait(pe, norm_ready, i, 2, g + 1)
                wait(pe, result_ready, i, 2, g - 2)
                wait(pe, q_lo_ready, i, 2, g)
                for t in range(TILES):
                    mm = pe.transpose(ps_misc[:, t * P:(t + 1) * P], x_norm[:, g % 2, t, :], ident[:])
                mm.then_inc(hT_ready, 1)

            def project_q(i, g):
                wait(pe, hT_copied, i, 2, g + 1)
                pe.matmul(ps_misc[:, ROWS:2 * ROWS], w_sb[:], hT[:], start=True, stop=True).then_inc(qT_ready, 1)

            def scores(i, k):
                slot, half = k // 2 % 2, k % 2
                if half == 0:
                    wait(pe, masked, i, BODY // 2, k // 2 - 1)
                if k % GROUP_STEPS == 0:
                    wait(pe, q_lo_ready, i, 2, k // GROUP_STEPS + 1)
                g, t, c = k // GROUP_STEPS % 2, k // CHUNKS % TILES, k % CHUNKS
                for n, (qp, kp) in enumerate(((0, 0), (0, 1), (1, 0))):
                    mm = pe.matmul(ps_scores[:, slot, half * CHUNK:(half + 1) * CHUNK],
                                   qT[qp][:, g, t * P:(t + 1) * P], kT[kp][:, c * CHUNK:(c + 1) * CHUNK],
                                   start=(n == 0), stop=(n == 2))
                if half == 1:
                    mm.then_inc(scores_ready, 1)

            def turn(i, k):
                g, j = k // GROUP_STEPS, k % GROUP_STEPS
                if j % 4 == 0:
                    wait(pe, probs_ready, i, BODY // 2, PAIRS * (TILES * g + 1) + j // 4 + 1)
                wait(pe, lo_ready, i, BODY, k - 1)
                for b in range(2):
                    for t in range(TILES):
                        at = (b * TILES + t) * P
                        col = (2 * j + b) * P
                        mm = pe.transpose(ps_turn[:, k % 2, at:at + P],
                                          probs[:, (TILES * g + t) % SLOTS, col:col + P], ident[:])
                mm.then_inc(turned, 1)

            def weigh(i, k):
                g, j = k // GROUP_STEPS, k % GROUP_STEPS
                wait(pe, lo_ready, i, BODY, k + 1)
                if j == 0:
                    wait(pe, acc_copied, i, 2, g)
                r = k % PART_RING
                for b in range(2):
                    for n, (v, p) in enumerate(((0, part_hi), (1, part_hi), (0, part_lo))):
                        mm = pe.matmul(ps_acc[:, 0:ROWS], val[v][:, 2 * j + b, :],
                                       p[:, r, b * ROWS:(b + 1) * ROWS],
                                       start=(j == 0 and b == 0 and n == 0),
                                       stop=(j == GROUP_STEPS - 1 and b == 1 and n == 2))
                mm.then_inc(weighed, 1)

            def turn_back(i, g):
                wait(pe, acc_copied, i, 2, g + 1)
                for t in range(TILES):
                    mm = pe.transpose(ps_misc[:, t * P:(t + 1) * P], accT_sb[:, t * P:(t + 1) * P], ident[:])
                mm.then_inc(acc_turned, 1)

            pe.wait_ge(ident_ready, 1)
            turn_h(0, 0)
            pe.wait_ge(w_landed, 16)
            project_q(0, 0)

            def step(i, s):
                if isinstance(i, int) and i == 0:
                    for c in ((0, 1, 2) if s == 0 else (s + 2,)):
                        if c < CHUNKS:
                            if c % 3 == 0:
                                pe.wait_ge(inp_landed[c // 3], 16)
                            turn_keys(c)
                    if s < CHUNKS:
                        pe.wait_ge(k_lo_ready, s + 1)
                if live(i, s, BODY, STEPS):
                    scores(i, s)
                if live(i, s - LAG, BODY, STEPS):
                    turn(i, s - LAG)
                if live(i, s - LAG - WEIGH, BODY, STEPS):
                    if isinstance(i, int) and i == 0 and s == LAG + WEIGH:
                        pe.wait_ge(v_lo_ready, 1)
                    weigh(i, s - LAG - WEIGH)
                g = s // GROUP_STEPS
                if s % GROUP_STEPS == 7 and live(i, g - 2, 2, GROUPS):
                    turn_back(i, g - 2)
                if s % GROUP_STEPS == 12 and live(i, g + 1, 2, GROUPS):
                    turn_h(i, g + 1)
                if s % GROUP_STEPS == 14 and live(i, g + 1, 2, GROUPS):
                    project_q(i, g + 1)

            run(pe, step)

        @block.scalar
        def _(act):
            def copy_h(i, g):
                wait(act, hT_ready, i, 2, g + 1)
                act.activation(hT[:], ps_misc[:, 0:ROWS], ACT.Relu).then_inc(hT_copied, 1)

            def take_q_hi(i, g):
                wait(act, qT_ready, i, 2, g + 1)
                wait(act, scores_ready, i, BODY // 2, (g - 1) * GROUP_STEPS // 2)
                act.activation(qT[0][:, g % 2, :], ps_misc[:, ROWS:2 * ROWS], ACT.Copy).then_inc(q_hi_ready, 1)

            def exponentiate(i, e):
                t, b = e // PAIRS, e % PAIRS
                if b == 0:
                    wait(act, exp_bias_ready, i, SLOTS, t + 1)
                    wait(act, sum_ready, i, 2, t // TILES - 1)
                v = probs[:, t % SLOTS, b * PAIR:(b + 1) * PAIR]
                act.activation(v, v, ACT.Exp, bias=exp_bias[:, t % SLOTS:t % SLOTS + 1], scale=1.0 / TEMPERATURE,
                               accum_out=part_sum[:, t % SLOTS, b:b + 1]).then_inc(probs_ready, 1)

            def take_hi(i, k):
                wait(act, turned, i, BODY, k + 1)
                wait(act, weighed, i, BODY, k - PART_RING + 1)
                act.activation(part_hi[:, k % PART_RING, :], ps_turn[:, k % 2, :], ACT.Copy).then_inc(hi_ready, 1)

            def copy_acc(i, g):
                wait(act, weighed, i, BODY, (g + 1) * GROUP_STEPS)
                wait(act, acc_turned, i, 2, g)
                act.activation(accT_sb[:], ps_acc[:, 0:ROWS], ACT.Copy).then_inc(acc_copied, 1)

            copy_h(0, 0)
            take_q_hi(0, 0)

            def step(i, s):
                if isinstance(i, int) and i == 0 and s < CHUNKS:
                    act.wait_ge(keys_turned, s + 1)
                    act.activation(kT[0][:, s * CHUNK:(s + 1) * CHUNK], ps_turn[:, s % 2, :], ACT.Copy)\
                        .then_inc(k_hi_ready, 1)
                if isinstance(i, int) and i == 0 and s == CHUNKS:
                    act.activation(val[0][:], inp_sb[:], ACT.Copy).then_inc(v_hi_ready, 1)
                g = s // GROUP_STEPS
                if s % GROUP_STEPS == 6 and live(i, g - 2, 2, GROUPS):
                    copy_acc(i, g - 2)
                if live(i, s - LAG, BODY, STEPS):
                    take_hi(i, s - LAG)
                if s % 2 == 1 and live(i, (s - EXP_AT) // 2, BODY // 2, STEPS // 2):
                    exponentiate(i, (s - EXP_AT) // 2)
                if s % GROUP_STEPS == 13 and live(i, g + 1, 2, GROUPS):
                    copy_h(i, g + 1)
                if s % GROUP_STEPS == 15 and live(i, g + 1, 2, GROUPS):
                    take_q_hi(i, g + 1)

            run(act, step)

        @block.vector
        def _(dve):
            def find_moments(i, g):
                wait(dve, x_landed[g % 2], i, 16, 16 * (g // 2 + 1))
                wait(dve, norm_ready, i, 2, g)
                for t in range(TILES):
                    dve.bn_stats(stats[:, t, :], x_norm[:, g % 2, t, :]).then_inc(stats_ready, 1)
                wait(dve, stats_ready, i, 2 * TILES, TILES * (g + 1))
                detach(dve)
                for t in range(TILES):
                    mm = dve.bn_aggr(moments[:, t, :], stats[:, t, :])
                mm.then_inc(moments_ready, 1)

            def normalise(i, g):
                wait(dve, rstd_ready, i, 2, g + 1)
                for t in range(TILES):
                    v = x_norm[:, g % 2, t, :]
                    mm = dve.tensor_scalar(v, v, moments[:, t, 0:1], rstd[:, t:t + 1], ALU.subtract, ALU.mult)
                mm.then_inc(norm_ready, 1)

            def take_q_lo(i, g):
                wait(dve, q_hi_ready, i, 2, g + 1)
                dve.tensor_tensor(qT[1][:, g % 2, :], ps_misc[:, ROWS:2 * ROWS], qT[0][:, g % 2, :],
                                  ALU.subtract).then_inc(q_lo_ready, 1)

            def mask(i, e):
                t, b = e // PAIRS, e % PAIRS
                wait(dve, scores_ready, i, BODY // 2, e + 1)
                if e % 2 == 0:
                    wait(dve, bias_ready, i, BODY_THIRDS, e // 2 + 1)
                wait(dve, turned, i, BODY, (t - SLOTS) // TILES * GROUP_STEPS + 4 * b + 4)
                detach(dve)
                dve.tensor_tensor_reduce(
                    probs[:, t % SLOTS, b * PAIR:(b + 1) * PAIR], ps_scores[:, e % 2, :],
                    bias[:, e // 2 % BIAS_RING, e % 2 * PAIR:(e % 2 + 1) * PAIR], 1.0, -3.0e38,
                    ALU.add, ALU.max, part_max[:, t % 2, b:b + 1]).then_inc(masked, 1)
                if b == PAIRS - 1:
                    wait(dve, masked, i, BODY // 2, e + 1)
                    dve.tensor_reduce(row_max[:, t % SLOTS:t % SLOTS + 1], part_max[:, t % 2, :], AX.X, ALU.max)\
                        .then_inc(max_found, 1)
                    wait(dve, max_found, i, SLOTS, t + 1)
                    dve.tensor_scalar(exp_bias[:, t % SLOTS:t % SLOTS + 1], row_max[:, t % SLOTS:t % SLOTS + 1],
                                      -1.0 / TEMPERATURE, LIFT, ALU.mult, ALU.add).then_inc(exp_bias_ready, 1)

            def take_lo(i, k):
                wait(dve, hi_ready, i, BODY, k + 1)
                dve.tensor_tensor(part_lo[:, k % PART_RING, :], ps_turn[:, k % 2, :], part_hi[:, k % PART_RING, :],
                                  ALU.subtract).then_inc(lo_ready, 1)

            def sum_rows(i, g):
                wait(dve, probs_ready, i, BODY // 2, (g + 1) * TILES * PAIRS)
                a = g * TILES % SLOTS
                dve.tensor_reduce(row_sum[:], part_sum[:, a:a + TILES, :], AX.X, ALU.add).then_inc(sum_ready, 1)
                wait(dve, sum_ready, i, 2, g + 1)
                dve.reciprocal(inv_sum[:], row_sum[:]).then_inc(inv_ready, 1)

            def finish(i, g):
                wait(dve, inv_ready, i, 2, g + 1)
                wait(dve, acc_turned, i, 2, g + 1)
                wait(dve, res_landed[g % 2], i, 16, 16 * (g // 2 + 1))
                wait(dve, stored[g % 2], i, 16, 16 * (g // 2))
                for t in range(TILES):
                    mm = dve.scalar_tensor_tensor(out=result[:, g % 2, t, :], in0=ps_misc[:, t * P:(t + 1) * P],
                                                  scalar=inv_sum[:, t:t + 1], in1=x_res[:, g % 2, t, :],
                                                  op0=ALU.mult, op1=ALU.add)
                mm.then_inc(result_ready, 1)

            find_moments(0, 0)
            normalise(0, 0)
            take_q_lo(0, 0)

            def step(i, s):
                if isinstance(i, int) and i == 0 and s < CHUNKS:
                    dve.wait_ge(k_hi_ready, s + 1)
                    at = slice(s * CHUNK, (s + 1) * CHUNK)
                    dve.tensor_tensor(kT[1][:, at], ps_turn[:, s % 2, :], kT[0][:, at], ALU.subtract)\
                        .then_inc(k_lo_ready, 1)
                if isinstance(i, int) and i == 0 and s == 2 * CHUNKS:
                    dve.wait_ge(v_hi_ready, 1)
                    dve.tensor_tensor(val[1][:], inp_sb[:], val[0][:], ALU.subtract).then_inc(v_lo_ready, 1)
                    dve.wait_ge(v_lo_ready, 1)
                g = s // GROUP_STEPS
                if s % 2 == 0 and live(i, s // 2 - 1, BODY // 2, STEPS // 2):
                    mask(i, s // 2 - 1)
                if live(i, s - LAG, BODY, STEPS):
                    take_lo(i, s - LAG)
                if s % GROUP_STEPS == 1 and live(i, g + 1, 2, GROUPS):
                    find_moments(i, g + 1)
                if s % GROUP_STEPS == 5 and live(i, g - 2, 2, GROUPS):
                    sum_rows(i, g - 2)
                if s % GROUP_STEPS == 8 and live(i, g - 2, 2, GROUPS):
                    finish(i, g - 2)
                if s % GROUP_STEPS == 11 and live(i, g + 1, 2, GROUPS):
                    normalise(i, g + 1)
                if s % GROUP_STEPS == 16 and live(i, g + 1, 2, GROUPS):
                    take_q_lo(i, g + 1)

            run(dve, step)


_INS = ["x", "adj", "L0_gnn_input", "L0_gnn_weight"]


def kernel(**inputs):
    import numpy as _np
    import concourse.bacc as _bacc
    from concourse import mybir as _mybir
    from concourse.bass_utils import run_bass_kernel_spmd as _run

    nc = _bacc.Bacc("TRN2", target_bir_lowering=False, num_devices=1)
    arrays, args = {}, []
    for name in _INS:
        a = _np.ascontiguousarray(inputs[name])
        arrays[f"in_{name}_dram"] = a
        args.append(nc.dram_tensor(f"in_{name}_dram", a.shape, _mybir.dt.from_np(a.dtype), kind="ExternalInput").ap())
    out = nc.dram_tensor("out_dram", inputs["x"].shape, _mybir.dt.float32, kind="ExternalOutput").ap()
    adjacency_attention(nc, *args, out)
    r = _run(nc, [arrays], core_ids=[0])
    return r.results[0]["out_dram"]
```

```python
from contextlib import ExitStack

import concourse.bass as bass
from concourse import mybir

ALU = mybir.AluOpType
ACT = mybir.ActivationFunctionType
AX = mybir.AxisListType
F32 = mybir.dt.float32
F16 = mybir.dt.float16
BF16 = mybir.dt.bfloat16
I32 = mybir.dt.int32

P = 128
TEMPERATURE = 0.07000000029802322
EPS = 1e-5
BIG = 2.0 ** 60
NO_EDGE = -BIG / 4
TINY = 1e-30
LIFT = 9.0

CHUNK = 512
PAIR = 2 * CHUNK
THIRD = 2048
TILES = 2
ROWS = TILES * P
ADJ_RING, PENALTY_RING, PART_RING = 4, 4, 4

LAG = 29
WEIGH = 2
EXP_AT = 15


def adjacency_attention(nc, x, adj, inp, weight, out):
    M, D = x.shape
    N = inp.shape[0]
    assert D == P and adj.shape == (M, N)
    CHUNKS = N // CHUNK
    PAIRS = N // PAIR
    THIRDS = N // THIRD
    BLOCKS = N // P
    GROUP_STEPS = TILES * CHUNKS
    BODY = 2 * GROUP_STEPS
    SLOTS = BODY // CHUNKS
    STEPS = M // P * CHUNKS
    GROUPS = M // ROWS
    BODIES = STEPS // BODY
    assert STEPS % BODY == 0 and 2 * GROUP_STEPS == BLOCKS
    END = (LAG + WEIGH) % GROUP_STEPS
    TAIL = LAG + WEIGH + 5
    BODY_THIRDS = SLOTS * THIRDS

    inp_view = inp.rearrange("(b p) d -> p b d", p=P)
    x_view = x.rearrange("(g t p) d -> p g t d", p=P, t=TILES)
    out_view = out.rearrange("(g t p) d -> p g t d", p=P, t=TILES)
    adj_view = adj.rearrange("(t p) n -> p t n", p=P)

    with ExitStack() as ctx:
        def sb(name, shape, dt):
            return ctx.enter_context(nc.sbuf_tensor(name, shape, dt))

        def psum(name, shape):
            return ctx.enter_context(nc.psum_tensor(name, shape, F32))

        def sem(name):
            return ctx.enter_context(nc.semaphore(name))

        probs = sb("probs", [P, SLOTS, N], F32)
        kT = [sb("kT_hi", [P, N], F16), sb("kT_lo", [P, N], F16)]
        val = [sb("val_hi", [P, BLOCKS, D], F16), sb("val_lo", [P, BLOCKS, D], F16)]
        adj_sb = sb("adj_sb", [P, ADJ_RING, THIRD], I32)
        penalty = sb("penalty", [P, PENALTY_RING, PAIR], BF16)
        part_hi = sb("part_hi", [P, PART_RING, CHUNK], F16)
        part_lo = sb("part_lo", [P, PART_RING, CHUNK], F16)
        qT = [sb("qT_hi", [P, 2, ROWS], F16), sb("qT_lo", [P, 2, ROWS], F16)]
        ident = sb("ident", [P, P], F32)
        w_sb = sb("w_sb", [P, D], F32)
        x_norm = sb("x_norm", [P, 2, TILES, D], F32)
        x_res = sb("x_res", [P, 2, TILES, D], F32)
        stats = sb("stats", [P, TILES, 6], F32)
        moments = sb("moments", [P, TILES, 2], F32)
        var_eps = sb("var_eps", [P, TILES], F32)
        rstd = sb("rstd", [P, TILES], F32)
        minus_half = sb("minus_half", [P, TILES], F32)
        hT = sb("hT", [P, ROWS], F32)
        part_max = sb("part_max", [P, 2, PAIRS], F32)
        row_max = sb("row_max", [P, SLOTS], F32)
        exp_bias = sb("exp_bias", [P, SLOTS], F32)
        part_sum = sb("part_sum", [P, SLOTS, PAIRS + 1], F32)
        row_sum = sb("row_sum", [P, 2, TILES], F32)
        no_edges = sb("no_edges", [P, TILES], F32)
        val_sum = sb("val_sum", [P, D], F32)
        val_mean = sb("val_mean", [P, D], F32)
        big = sb("big", [P, 1], F32)
        ones = sb("ones", [P, P], F32)
        mean_part = sb("mean_part", [P, TILES, D], F32)
        inv_sum = sb("inv_sum", [P, 2, TILES], F32)
        accT_sb = sb("accT_sb", [P, ROWS], F32)
        result = sb("result", [P, 2, TILES, D], F32)
        inp_sb = probs[:, SLOTS - 1, :].rearrange("p (b d) -> p b d", d=D)

        ps_scores = psum("ps_scores", [P, 2, PAIR])
        ps_turn = psum("ps_turn", [P, 2, CHUNK])
        ps_acc = psum("ps_acc", [P, CHUNK])
        ps_misc = psum("ps_misc", [P, CHUNK])

        inp_landed = [sem(f"inp_landed{c}") for c in range(4)]
        w_landed = sem("w_landed")
        x_landed = [sem(f"x_landed{c}") for c in range(2)]
        res_landed = [sem(f"res_landed{c}") for c in range(2)]
        adj_landed = [sem(f"adj_landed{c}") for c in range(ADJ_RING)]
        stored = [sem(f"stored{c}") for c in range(2)]
        wait_over = [sem("wait_over_vector"), sem("wait_over_gpsimd")]
        ident_blank = sem("ident_blank")
        ident_ready = sem("ident_ready")
        big_ready = sem("big_ready")
        half_ready = sem("half_ready")
        ones_ready = sem("ones_ready")
        tiny_ready = sem("tiny_ready")
        val_sum_ready = sem("val_sum_ready")
        mean_summed = sem("mean_summed")
        mean_ready = sem("mean_ready")
        even_penalty_ready = sem("even_penalty_ready")
        odd_penalty_ready = sem("odd_penalty_ready")
        no_edges_found = sem("no_edges_found")
        mean_part_ready = sem("mean_part_ready")
        res_ready = sem("res_ready")
        var_ready = sem("var_ready")
        rstd_ready = sem("rstd_ready")
        stats_ready = sem("stats_ready")
        moments_ready = sem("moments_ready")
        norm_ready = sem("norm_ready")
        hT_ready = sem("hT_ready")
        hT_copied = sem("hT_copied")
        qT_ready = sem("qT_ready")
        q_hi_ready = sem("q_hi_ready")
        q_lo_ready = sem("q_lo_ready")
        keys_turned = sem("keys_turned")
        k_hi_ready = sem("k_hi_ready")
        k_lo_ready = sem("k_lo_ready")
        v_hi_ready = sem("v_hi_ready")
        v_lo_ready = sem("v_lo_ready")
        scores_ready = sem("scores_ready")
        masked = sem("masked")
        max_found = sem("max_found")
        exp_bias_ready = sem("exp_bias_ready")
        probs_ready = sem("probs_ready")
        turned = sem("turned")
        hi_ready = sem("hi_ready")
        lo_ready = sem("lo_ready")
        weighed = sem("weighed")
        acc_copied = sem("acc_copied")
        acc_turned = sem("acc_turned")
        sum_ready = sem("sum_ready")
        inv_ready = sem("inv_ready")
        result_ready = sem("result_ready")

        def live(i, k, per_body, last):
            return not isinstance(i, int) or 0 <= per_body * i + k < last

        def wait(eng, semaphore, i, per_body, count):
            if not isinstance(i, int):
                eng.wait_ge(semaphore, i * per_body + count)
            elif per_body * i + count > 0:
                eng.wait_ge(semaphore, per_body * i + count)

        def detach(eng):
            eng.sem_inc(wait_over[eng is nc.gpsimd], 1)

        def group_of(view, i, g):
            if isinstance(i, int):
                return view[:, 2 * i + g]
            return view[:, bass.ds(i * 2 + g, 1)].rearrange("p o t d -> p (o t) d")

        def run(eng, step):
            for s in range(BODY):
                step(0, s)
            with eng.Fori(1, BODIES - 1) as i:
                for s in range(BODY):
                    step(i, s)
            for s in range(BODY + TAIL):
                step(BODIES - 1, s)

        block = ctx.enter_context(nc.Block())

        @block.sync
        def _(sp):
            def load_adj(i, r):
                wait(sp, even_penalty_ready, i, BODY_THIRDS, r - ADJ_RING + 1)
                wait(sp, odd_penalty_ready, i, BODY_THIRDS, r - ADJ_RING + 1)
                tile = i * SLOTS + r // THIRDS
                c = r % THIRDS * THIRD
                sp.dma_start(adj_sb[:, r % ADJ_RING, :],
                             adj_view[:, tile, c:c + THIRD] if isinstance(i, int) else
                             adj_view[:, bass.ds(tile, 1), c:c + THIRD].rearrange("p o n -> p (o n)"))\
                    .then_inc(adj_landed[r % ADJ_RING], 16)

            def load_x(i, g):
                wait(sp, hT_ready, i, 2, g - 1)
                sp.dma_start(x_norm[:, g % 2], group_of(x_view, i, g)).then_inc(x_landed[g % 2], 16)

            def load_res(i, g):
                wait(sp, result_ready, i, 2, g - 1)
                sp.dma_start(x_res[:, g % 2], group_of(x_view, i, g)).then_inc(res_landed[g % 2], 16)

            load_x(0, 0)
            sp.dma_start(w_sb[:], weight).then_inc(w_landed, 16)
            part = BLOCKS // 4
            for c in range(4):
                sp.dma_start(inp_sb[:, c * part:(c + 1) * part, :], inp_view[:, c * part:(c + 1) * part, :])\
                    .then_inc(inp_landed[c], 16)

            def step(i, s):
                if s % 4 == 0 and live(i, s // 4, BODY_THIRDS, STEPS // 4):
                    load_adj(i, s // 4)
                g = s // GROUP_STEPS
                if s % GROUP_STEPS == 4 and live(i, g + 1, 2, GROUPS):
                    load_x(i, g + 1)
                if s % GROUP_STEPS == 10 and live(i, g - 1, 2, GROUPS):
                    load_res(i, g - 1)

            run(sp, step)
            for c in range(2):
                sp.wait_ge(stored[c], 16 * GROUPS // 2)

        @block.gpsimd
        def _(pool):
            pool.memset(minus_half[:], -0.5).then_inc(half_ready, 1)
            pool.memset(big[:], BIG).then_inc(big_ready, 1)
            pool.memset(ident[:], 0.0).then_inc(ident_blank, 1)
            pool.wait_ge(ident_blank, 1)
            pool.affine_select(out=ident[:], in_=ident[:], compare_op=ALU.not_equal, fill=1.0, base=0,
                               pattern=[[-1, P]], channel_multiplier=1).then_inc(ident_ready, 1)
            pool.wait_ge(half_ready, 1)

            def invert_deviation(i, g):
                wait(pool, moments_ready, i, 2, g + 1)
                wait(pool, norm_ready, i, 2, g)
                detach(pool)
                pool.tensor_scalar(var_eps[:], moments[:, :, 1], EPS, None, ALU.add).then_inc(var_ready, 1)
                wait(pool, var_ready, i, 2, g + 1)
                pool.tensor_tensor(rstd[:], var_eps[:], minus_half[:], ALU.pow).then_inc(rstd_ready, 1)

            invert_deviation(0, 0)

            def normalise(i, g):
                wait(pool, rstd_ready, i, 2, g + 1)
                detach(pool)
                for t in range(TILES):
                    v = x_norm[:, g % 2, t, :]
                    mm = pool.tensor_scalar(v, v, moments[:, t, 0:1], rstd[:, t:t + 1], ALU.subtract, ALU.mult)
                mm.then_inc(norm_ready, 1)

            def odd_penalty(i, r):
                e = 2 * r + 1
                wait(pool, adj_landed[r % ADJ_RING], i, 16 * BODY_THIRDS // ADJ_RING, 16 * (r // ADJ_RING + 1))
                wait(pool, masked, i, BODY // 2, e - PENALTY_RING + 1)
                detach(pool)
                pool.tensor_scalar(penalty[:, e % PENALTY_RING, :], adj_sb[:, r % ADJ_RING, PAIR:THIRD], 0.0, BIG,
                                   ALU.is_le, ALU.mult).then_inc(odd_penalty_ready, 1)

            def give_mean(i, g):
                wait(pool, sum_ready, i, 2, g + 1)
                detach(pool)
                pool.tensor_scalar(no_edges[:], row_sum[:, g % 2, :], 1.0, None, ALU.is_le)\
                    .then_inc(no_edges_found, 1)
                wait(pool, no_edges_found, i, 2, g + 1)
                detach(pool)
                for t in range(TILES):
                    mm = pool.tensor_scalar(mean_part[:, t, :], val_mean[:], no_edges[:, t:t + 1], None, ALU.mult)
                mm.then_inc(mean_part_ready, 1)
                wait(pool, mean_part_ready, i, 2, g + 1)
                wait(pool, res_landed[g % 2], i, 16, 16 * (g // 2 + 1))
                pool.tensor_tensor(x_res[:, g % 2], x_res[:, g % 2], mean_part[:], ALU.add).then_inc(res_ready, 1)

            normalise(0, 0)
            pool.memset(ones[:], 1.0).then_inc(ones_ready, 1)
            pool.memset(part_sum[:, :, PAIRS:], TINY).then_inc(tiny_ready, 1)

            def step(i, s):
                if s % 4 == 0 and live(i, s // 4, BODY_THIRDS, STEPS // 4):
                    odd_penalty(i, s // 4)
                g = s // GROUP_STEPS
                if s % GROUP_STEPS == 4 and live(i, g + 1, 2, GROUPS):
                    invert_deviation(i, g + 1)
                    normalise(i, g + 1)
                if s % GROUP_STEPS == 16 and live(i, g - 1, 2, GROUPS):
                    if isinstance(i, int) and i == 0 and g == 1:
                        pool.wait_ge(mean_ready, 1)
                    give_mean(i, g - 1)

            run(pool, step)

        @block.tensor
        def _(pe):
            def turn_keys(c):
                if c >= 2:
                    pe.wait_ge(k_lo_ready, c - 1)
                for b in range(4):
                    mm = pe.transpose(ps_turn[:, c % 2, b * P:(b + 1) * P], inp_sb[:, 4 * c + b, :], ident[:])
                mm.then_inc(keys_turned, 1)

            def turn_h(i, g):
                wait(pe, norm_ready, i, 2, g + 1)
                wait(pe, result_ready, i, 2, g - 2)
                wait(pe, q_lo_ready, i, 2, g)
                if isinstance(i, int) and i == 0 and g == 2:
                    pe.wait_ge(mean_ready, 1)
                for t in range(TILES):
                    mm = pe.transpose(ps_misc[:, t * P:(t + 1) * P], x_norm[:, g % 2, t, :], ident[:])
                mm.then_inc(hT_ready, 1)

            def project_q(i, g):
                wait(pe, hT_copied, i, 2, g + 1)
                pe.matmul(ps_misc[:, ROWS:2 * ROWS], w_sb[:], hT[:], start=True, stop=True).then_inc(qT_ready, 1)

            def sum_values():
                pe.wait_ge(val_sum_ready, 1)
                pe.wait_ge(ones_ready, 1)
                pe.wait_ge(q_lo_ready, 2)
                pe.matmul(ps_misc[:, 0:D], ones[:], val_sum[:], start=True, stop=True).then_inc(mean_summed, 1)

            def scores(i, k):
                slot, half = k // 2 % 2, k % 2
                if half == 0:
                    wait(pe, masked, i, BODY // 2, k // 2 - 1)
                if k % GROUP_STEPS == 0:
                    wait(pe, q_lo_ready, i, 2, k // GROUP_STEPS + 1)
                g, t, c = k // GROUP_STEPS % 2, k // CHUNKS % TILES, k % CHUNKS
                for n, (qp, kp) in enumerate(((0, 0), (0, 1), (1, 0))):
                    mm = pe.matmul(ps_scores[:, slot, half * CHUNK:(half + 1) * CHUNK],
                                   qT[qp][:, g, t * P:(t + 1) * P], kT[kp][:, c * CHUNK:(c + 1) * CHUNK],
                                   start=(n == 0), stop=(n == 2))
                if half == 1:
                    mm.then_inc(scores_ready, 1)

            def turn(i, k):
                g, j = k // GROUP_STEPS, k % GROUP_STEPS
                if j % 4 == 0:
                    wait(pe, probs_ready, i, BODY // 2, PAIRS * (TILES * g + 1) + j // 4 + 1)
                wait(pe, lo_ready, i, BODY, k - 1)
                for b in range(2):
                    for t in range(TILES):
                        at = (b * TILES + t) * P
                        col = (2 * j + b) * P
                        mm = pe.transpose(ps_turn[:, k % 2, at:at + P],
                                          probs[:, (TILES * g + t) % SLOTS, col:col + P], ident[:])
                mm.then_inc(turned, 1)

            def weigh(i, k):
                g, j = k // GROUP_STEPS, k % GROUP_STEPS
                wait(pe, lo_ready, i, BODY, k + 1)
                if j == 0:
                    wait(pe, acc_copied, i, 2, g)
                r = k % PART_RING
                for b in range(2):
                    for n, (v, p) in enumerate(((0, part_hi), (1, part_hi), (0, part_lo))):
                        mm = pe.matmul(ps_acc[:, 0:ROWS], val[v][:, 2 * j + b, :],
                                       p[:, r, b * ROWS:(b + 1) * ROWS],
                                       start=(j == 0 and b == 0 and n == 0),
                                       stop=(j == GROUP_STEPS - 1 and b == 1 and n == 2))
                mm.then_inc(weighed, 1)

            def turn_back(i, g):
                wait(pe, acc_copied, i, 2, g + 1)
                for t in range(TILES):
                    mm = pe.transpose(ps_misc[:, t * P:(t + 1) * P], accT_sb[:, t * P:(t + 1) * P], ident[:])
                mm.then_inc(acc_turned, 1)

            pe.wait_ge(ident_ready, 1)
            turn_h(0, 0)
            pe.wait_ge(w_landed, 16)
            project_q(0, 0)

            def step(i, s):
                if isinstance(i, int) and i == 0:
                    for c in ((0, 1, 2) if s == 0 else (s + 2,)):
                        if c < CHUNKS:
                            if c % 3 == 0:
                                pe.wait_ge(inp_landed[c // 3], 16)
                            turn_keys(c)
                    if s < CHUNKS:
                        pe.wait_ge(k_lo_ready, s + 1)
                if live(i, s, BODY, STEPS):
                    scores(i, s)
                k = s - LAG - WEIGH
                if (k - 1) % GROUP_STEPS == 0 and live(i, k - 1, BODY, STEPS):
                    if isinstance(i, int) and i == 0:
                        pe.wait_ge(v_lo_ready, 1)
                    weigh(i, k - 1)
                if live(i, s - LAG, BODY, STEPS):
                    turn(i, s - LAG)
                if k % GROUP_STEPS != 0 and live(i, k, BODY, STEPS):
                    weigh(i, k)
                if isinstance(i, int) and i == 0 and s == 22:
                    sum_values()
                g = s // GROUP_STEPS
                if s % GROUP_STEPS == END + 1 and live(i, g - 2, 2, GROUPS):
                    turn_back(i, g - 2)
                if s % GROUP_STEPS == 12 and live(i, g + 1, 2, GROUPS):
                    turn_h(i, g + 1)
                if s % GROUP_STEPS == 14 and live(i, g + 1, 2, GROUPS):
                    project_q(i, g + 1)

            run(pe, step)

        @block.scalar
        def _(act):
            def copy_h(i, g):
                wait(act, hT_ready, i, 2, g + 1)
                act.activation(hT[:], ps_misc[:, 0:ROWS], ACT.Relu).then_inc(hT_copied, 1)

            def take_q_hi(i, g):
                wait(act, qT_ready, i, 2, g + 1)
                wait(act, scores_ready, i, BODY // 2, (g - 1) * GROUP_STEPS // 2)
                act.activation(qT[0][:, g % 2, :], ps_misc[:, ROWS:2 * ROWS], ACT.Copy).then_inc(q_hi_ready, 1)

            def even_penalty(i, r):
                e = 2 * r
                wait(act, adj_landed[r % ADJ_RING], i, 16 * BODY_THIRDS // ADJ_RING, 16 * (r // ADJ_RING + 1))
                wait(act, masked, i, BODY // 2, e - PENALTY_RING + 1)
                act.activation(penalty[:, e % PENALTY_RING, :], adj_sb[:, r % ADJ_RING, 0:PAIR], ACT.Relu,
                               scale=-BIG, bias=big[:]).then_inc(even_penalty_ready, 1)

            def exponentiate(i, e):
                t, b = e // PAIRS, e % PAIRS
                if b == 0:
                    wait(act, max_found, i, SLOTS, t + 1)
                    act.activation(exp_bias[:, t % SLOTS:t % SLOTS + 1], row_max[:, t % SLOTS:t % SLOTS + 1],
                                   ACT.Copy, bias=LIFT, scale=-1.0 / TEMPERATURE).then_inc(exp_bias_ready, 1)
                    wait(act, exp_bias_ready, i, SLOTS, t + 1)
                    wait(act, sum_ready, i, 2, t // TILES - 1)
                v = probs[:, t % SLOTS, b * PAIR:(b + 1) * PAIR]
                act.activation(v, v, ACT.Exp, bias=exp_bias[:, t % SLOTS:t % SLOTS + 1], scale=1.0 / TEMPERATURE,
                               accum_out=part_sum[:, t % SLOTS, b:b + 1]).then_inc(probs_ready, 1)

            def take_hi(i, k):
                wait(act, turned, i, BODY, k + 1)
                wait(act, weighed, i, BODY, k - PART_RING + 1)
                act.activation(part_hi[:, k % PART_RING, :], ps_turn[:, k % 2, :], ACT.Copy).then_inc(hi_ready, 1)

            def copy_acc(i, g):
                wait(act, weighed, i, BODY, (g + 1) * GROUP_STEPS)
                wait(act, acc_turned, i, 2, g)
                act.activation(accT_sb[:], ps_acc[:, 0:ROWS], ACT.Copy).then_inc(acc_copied, 1)

            def store(i, g):
                wait(act, result_ready, i, 2, g + 1)
                act.dma_start(group_of(out_view, i, g), result[:, g % 2]).then_inc(stored[g % 2], 16)

            copy_h(0, 0)
            take_q_hi(0, 0)
            act.wait_ge(big_ready, 1)
            even_penalty(0, 0)

            def step(i, s):
                if isinstance(i, int) and i == 0 and s < CHUNKS:
                    act.wait_ge(keys_turned, s + 1)
                    act.activation(kT[0][:, s * CHUNK:(s + 1) * CHUNK], ps_turn[:, s % 2, :], ACT.Copy)\
                        .then_inc(k_hi_ready, 1)
                if isinstance(i, int) and i == 0 and s == CHUNKS:
                    act.activation(val[0][:], inp_sb[:], ACT.Copy).then_inc(v_hi_ready, 1)
                g = s // GROUP_STEPS
                if s % GROUP_STEPS == END and live(i, g - 2, 2, GROUPS):
                    copy_acc(i, g - 2)
                if live(i, s - LAG, BODY, STEPS):
                    take_hi(i, s - LAG)
                if s % 4 == 2 and live(i, s // 4 + 1, BODY_THIRDS, STEPS // 4):
                    even_penalty(i, s // 4 + 1)
                if isinstance(i, int) and i == 0 and s == 23:
                    act.wait_ge(mean_summed, 1)
                    act.activation(val_mean[:], ps_misc[:, 0:D], ACT.Copy, scale=1.0 / N).then_inc(mean_ready, 1)
                if s % 2 == 1 and live(i, (s - EXP_AT) // 2, BODY // 2, STEPS // 2):
                    exponentiate(i, (s - EXP_AT) // 2)
                if s % GROUP_STEPS == END + 4 and live(i, g - 2, 2, GROUPS):
                    store(i, g - 2)
                if s % GROUP_STEPS == 13 and live(i, g + 1, 2, GROUPS):
                    copy_h(i, g + 1)
                if s % GROUP_STEPS == 15 and live(i, g + 1, 2, GROUPS):
                    take_q_hi(i, g + 1)

            run(act, step)

        @block.vector
        def _(dve):
            def find_moments(i, g):
                wait(dve, x_landed[g % 2], i, 16, 16 * (g // 2 + 1))
                wait(dve, norm_ready, i, 2, g)
                for t in range(TILES):
                    dve.bn_stats(stats[:, t, :], x_norm[:, g % 2, t, :]).then_inc(stats_ready, 1)
                wait(dve, stats_ready, i, 2 * TILES, TILES * (g + 1))
                detach(dve)
                for t in range(TILES):
                    mm = dve.bn_aggr(moments[:, t, :], stats[:, t, :])
                mm.then_inc(moments_ready, 1)

            def take_q_lo(i, g):
                wait(dve, q_hi_ready, i, 2, g + 1)
                dve.tensor_tensor(qT[1][:, g % 2, :], ps_misc[:, ROWS:2 * ROWS], qT[0][:, g % 2, :],
                                  ALU.subtract).then_inc(q_lo_ready, 1)

            def mask(i, e):
                t, b = e // PAIRS, e % PAIRS
                wait(dve, scores_ready, i, BODY // 2, e + 1)
                wait(dve, (even_penalty_ready, odd_penalty_ready)[e % 2], i, BODY_THIRDS, e // 2 + 1)
                wait(dve, turned, i, BODY, (t - SLOTS) // TILES * GROUP_STEPS + 4 * b + 4)
                detach(dve)
                dve.tensor_tensor_reduce(
                    probs[:, t % SLOTS, b * PAIR:(b + 1) * PAIR], ps_scores[:, e % 2, :],
                    penalty[:, e % PENALTY_RING, :], 1.0, NO_EDGE, ALU.subtract, ALU.max, part_max[:, t % 2, b:b + 1]).then_inc(masked, 1)
                if b == PAIRS - 1:
                    wait(dve, masked, i, BODY // 2, e + 1)
                    dve.tensor_reduce(row_max[:, t % SLOTS:t % SLOTS + 1], part_max[:, t % 2, :], AX.X, ALU.max)\
                        .then_inc(max_found, 1)

            def take_lo(i, k):
                wait(dve, hi_ready, i, BODY, k + 1)
                dve.tensor_tensor(part_lo[:, k % PART_RING, :], ps_turn[:, k % 2, :], part_hi[:, k % PART_RING, :],
                                  ALU.subtract).then_inc(lo_ready, 1)

            def sum_rows(i, g):
                wait(dve, probs_ready, i, BODY // 2, (g + 1) * TILES * PAIRS)
                wait(dve, res_ready, i, 2, g - 1)
                wait(dve, result_ready, i, 2, g - 1)
                if isinstance(i, int):
                    dve.wait_ge(tiny_ready, 1)
                a = g * TILES % SLOTS
                dve.tensor_reduce(row_sum[:, g % 2, :], part_sum[:, a:a + TILES, :], AX.X, ALU.add).then_inc(sum_ready, 1)
                wait(dve, sum_ready, i, 2, g + 1)
                dve.reciprocal(inv_sum[:, g % 2, :], row_sum[:, g % 2, :]).then_inc(inv_ready, 1)

            def finish(i, g):
                wait(dve, inv_ready, i, 2, g + 1)
                wait(dve, acc_turned, i, 2, g + 1)
                wait(dve, res_ready, i, 2, g + 1)
                wait(dve, stored[g % 2], i, 16, 16 * (g // 2))
                for t in range(TILES):
                    mm = dve.scalar_tensor_tensor(out=result[:, g % 2, t, :], in0=ps_misc[:, t * P:(t + 1) * P],
                                                  scalar=inv_sum[:, g % 2, t:t + 1], in1=x_res[:, g % 2, t, :],
                                                  op0=ALU.mult, op1=ALU.add)
                mm.then_inc(result_ready, 1)

            find_moments(0, 0)
            take_q_lo(0, 0)

            def step(i, s):
                if isinstance(i, int) and i == 0 and s < CHUNKS:
                    dve.wait_ge(k_hi_ready, s + 1)
                    at = slice(s * CHUNK, (s + 1) * CHUNK)
                    dve.tensor_tensor(kT[1][:, at], ps_turn[:, s % 2, :], kT[0][:, at], ALU.subtract)\
                        .then_inc(k_lo_ready, 1)
                if isinstance(i, int) and i == 0 and s == 2 * CHUNKS:
                    dve.wait_ge(v_hi_ready, 1)
                    dve.tensor_tensor(val[1][:], inp_sb[:], val[0][:], ALU.subtract).then_inc(v_lo_ready, 1)
                    dve.wait_ge(v_lo_ready, 1)
                if isinstance(i, int) and i == 0 and s == 14:
                    dve.tensor_reduce(val_sum[:], inp_sb.rearrange("p b d -> p d b"), AX.X, ALU.add)\
                        .then_inc(val_sum_ready, 1)
                g = s // GROUP_STEPS
                if s % 2 == 0 and live(i, s // 2 - 1, BODY // 2, STEPS // 2):
                    mask(i, s // 2 - 1)
                if live(i, s - LAG, BODY, STEPS):
                    take_lo(i, s - LAG)
                if s % GROUP_STEPS == 1 and live(i, g + 1, 2, GROUPS):
                    find_moments(i, g + 1)
                if s % GROUP_STEPS == 15 and live(i, g - 1, 2, GROUPS):
                    sum_rows(i, g - 1)
                if s % GROUP_STEPS == END + 2 and live(i, g - 2, 2, GROUPS):
                    finish(i, g - 2)
                if s % GROUP_STEPS == 16 and live(i, g + 1, 2, GROUPS):
                    take_q_lo(i, g + 1)

            run(dve, step)


_INS = ["x", "adj", "L0_gnn_input", "L0_gnn_weight"]


def kernel(**inputs):
    import numpy as _np
    import concourse.bacc as _bacc
    from concourse import mybir as _mybir
    from concourse.bass_utils import run_bass_kernel_spmd as _run

    nc = _bacc.Bacc("TRN2", target_bir_lowering=False, num_devices=1)
    arrays, args = {}, []
    for name in _INS:
        a = _np.ascontiguousarray(inputs[name])
        arrays[f"in_{name}_dram"] = a
        args.append(nc.dram_tensor(f"in_{name}_dram", a.shape, _mybir.dt.from_np(a.dtype), kind="ExternalInput").ap())
    out = nc.dram_tensor("out_dram", inputs["x"].shape, _mybir.dt.float32, kind="ExternalOutput").ap()
    adjacency_attention(nc, *args, out)
    r = _run(nc, [arrays], core_ids=[0])
    return r.results[0]["out_dram"]
```

```python
from contextlib import ExitStack

import concourse.bass as bass
from concourse import mybir

ALU = mybir.AluOpType
ACT = mybir.ActivationFunctionType
AX = mybir.AxisListType
F32 = mybir.dt.float32
F16 = mybir.dt.float16
BF16 = mybir.dt.bfloat16
I32 = mybir.dt.int32

P = 128
TEMPERATURE = 0.07000000029802322
EPS = 1e-5
BIG = 2.0 ** 60
NO_EDGE = -BIG / 4
TINY = 1e-30
LIFT = 9.0

CHUNK = 512
PAIR = 2 * CHUNK
THIRD = 2048
TILES = 2
ROWS = TILES * P
ADJ_RING, PENALTY_RING, PART_RING = 4, 4, 4

LAG = 30
WEIGH = 2
EXP_AT = 15
SUM_AT = 14


def adjacency_attention(nc, x, adj, inp, weight, out):
    M, D = x.shape
    N = inp.shape[0]
    assert D == P and adj.shape == (M, N)
    CHUNKS = N // CHUNK
    PAIRS = N // PAIR
    THIRDS = N // THIRD
    BLOCKS = N // P
    GROUP_STEPS = TILES * CHUNKS
    BODY = 2 * GROUP_STEPS
    SLOTS = BODY // CHUNKS
    STEPS = M // P * CHUNKS
    GROUPS = M // ROWS
    BODIES = STEPS // BODY
    assert STEPS % BODY == 0 and 2 * GROUP_STEPS == BLOCKS
    END = (LAG + WEIGH) % GROUP_STEPS
    TAIL = LAG + WEIGH + 5
    BODY_THIRDS = SLOTS * THIRDS

    inp_view = inp.rearrange("(b p) d -> p b d", p=P)
    x_view = x.rearrange("(g t p) d -> p g t d", p=P, t=TILES)
    out_view = out.rearrange("(g t p) d -> p g t d", p=P, t=TILES)
    adj_view = adj.rearrange("(t p) n -> p t n", p=P)

    with ExitStack() as ctx:
        def sb(name, shape, dt):
            return ctx.enter_context(nc.sbuf_tensor(name, shape, dt))

        def psum(name, shape):
            return ctx.enter_context(nc.psum_tensor(name, shape, F32))

        def sem(name):
            return ctx.enter_context(nc.semaphore(name))

        probs = sb("probs", [P, SLOTS, N], F32)
        kT = [sb("kT_hi", [P, N], F16), sb("kT_lo", [P, N], F16)]
        val = [sb("val_hi", [P, BLOCKS, D], F16), sb("val_lo", [P, BLOCKS, D], F16)]
        adj_sb = sb("adj_sb", [P, ADJ_RING, THIRD], I32)
        penalty = sb("penalty", [P, PENALTY_RING, PAIR], BF16)
        part_hi = sb("part_hi", [P, PART_RING, CHUNK], F16)
        part_lo = sb("part_lo", [P, PART_RING, CHUNK], F16)
        qT = [sb("qT_hi", [P, 2, ROWS], F16), sb("qT_lo", [P, 2, ROWS], F16)]
        ident = sb("ident", [P, P], F32)
        w_sb = sb("w_sb", [P, D], F32)
        x_norm = sb("x_norm", [P, 2, TILES, D], F32)
        x_res = sb("x_res", [P, 2, TILES, D], F32)
        stats = sb("stats", [P, TILES, 6], F32)
        moments = sb("moments", [P, TILES, 2], F32)
        var_eps = sb("var_eps", [P, TILES], F32)
        rstd = sb("rstd", [P, TILES], F32)
        minus_half = sb("minus_half", [P, TILES], F32)
        hT = sb("hT", [P, ROWS], F32)
        part_max = sb("part_max", [P, 2, PAIRS], F32)
        row_max = sb("row_max", [P, SLOTS], F32)
        exp_bias = sb("exp_bias", [P, SLOTS], F32)
        part_sum = sb("part_sum", [P, SLOTS, PAIRS + 1], F32)
        row_sum = sb("row_sum", [P, 2, TILES], F32)
        no_edges = sb("no_edges", [P, TILES], F32)
        val_mean = sb("val_mean", [P, D], F32)
        big = sb("big", [P, 1], F32)
        ones = sb("ones", [P, P], F16)
        mean_part = sb("mean_part", [P, TILES, D], F32)
        inv_sum = sb("inv_sum", [P, 2, TILES], F32)
        accT_sb = sb("accT_sb", [P, ROWS], F32)
        result = sb("result", [P, 2, TILES, D], F32)
        inp_sb = probs[:, SLOTS - 1, :].rearrange("p (b d) -> p b d", d=D)

        ps_scores = psum("ps_scores", [P, 2, PAIR])
        ps_turn = psum("ps_turn", [P, 2, CHUNK])
        ps_acc = psum("ps_acc", [P, CHUNK])
        ps_misc = psum("ps_misc", [P, CHUNK])

        inp_landed = [sem(f"inp_landed{c}") for c in range(4)]
        w_landed = sem("w_landed")
        x_landed = [sem(f"x_landed{c}") for c in range(2)]
        res_landed = [sem(f"res_landed{c}") for c in range(2)]
        adj_landed = [sem(f"adj_landed{c}") for c in range(ADJ_RING)]
        stored = [sem(f"stored{c}") for c in range(2)]
        wait_over = [sem("wait_over_vector"), sem("wait_over_gpsimd")]
        ident_blank = sem("ident_blank")
        ident_ready = sem("ident_ready")
        big_ready = sem("big_ready")
        half_ready = sem("half_ready")
        ones_ready = sem("ones_ready")
        tiny_ready = sem("tiny_ready")
        mean_summed = sem("mean_summed")
        mean_ready = sem("mean_ready")
        even_penalty_ready = sem("even_penalty_ready")
        odd_penalty_ready = sem("odd_penalty_ready")
        no_edges_found = sem("no_edges_found")
        mean_part_ready = sem("mean_part_ready")
        res_ready = sem("res_ready")
        var_ready = sem("var_ready")
        rstd_ready = sem("rstd_ready")
        stats_ready = sem("stats_ready")
        moments_ready = sem("moments_ready")
        norm_ready = sem("norm_ready")
        hT_ready = sem("hT_ready")
        hT_copied = sem("hT_copied")
        qT_ready = sem("qT_ready")
        q_hi_ready = sem("q_hi_ready")
        q_lo_ready = sem("q_lo_ready")
        keys_turned = sem("keys_turned")
        k_hi_ready = sem("k_hi_ready")
        k_lo_ready = sem("k_lo_ready")
        v_hi_ready = sem("v_hi_ready")
        v_lo_ready = sem("v_lo_ready")
        scores_ready = sem("scores_ready")
        masked = sem("masked")
        max_found = sem("max_found")
        exp_bias_ready = sem("exp_bias_ready")
        probs_ready = sem("probs_ready")
        turned = sem("turned")
        hi_ready = sem("hi_ready")
        lo_ready = sem("lo_ready")
        weighed = sem("weighed")
        acc_copied = sem("acc_copied")
        acc_turned = sem("acc_turned")
        sum_ready = sem("sum_ready")
        inv_ready = sem("inv_ready")
        result_ready = sem("result_ready")

        def live(i, k, per_body, last):
            return not isinstance(i, int) or 0 <= per_body * i + k < last

        def wait(eng, semaphore, i, per_body, count):
            if not isinstance(i, int):
                eng.wait_ge(semaphore, i * per_body + count)
            elif per_body * i + count > 0:
                eng.wait_ge(semaphore, per_body * i + count)

        def detach(eng):
            eng.sem_inc(wait_over[eng is nc.gpsimd], 1)

        def group_of(view, i, g):
            if isinstance(i, int):
                return view[:, 2 * i + g]
            return view[:, bass.ds(i * 2 + g, 1)].rearrange("p o t d -> p (o t) d")

        def run(eng, step):
            for s in range(BODY):
                step(0, s)
            with eng.Fori(1, BODIES - 1) as i:
                for s in range(BODY):
                    step(i, s)
            for s in range(BODY + TAIL):
                step(BODIES - 1, s)

        block = ctx.enter_context(nc.Block())

        @block.sync
        def _(sp):
            def load_adj(i, r):
                wait(sp, even_penalty_ready, i, BODY_THIRDS, r - ADJ_RING + 1)
                wait(sp, odd_penalty_ready, i, BODY_THIRDS, r - ADJ_RING + 1)
                tile = i * SLOTS + r // THIRDS
                c = r % THIRDS * THIRD
                sp.dma_start(adj_sb[:, r % ADJ_RING, :],
                             adj_view[:, tile, c:c + THIRD] if isinstance(i, int) else
                             adj_view[:, bass.ds(tile, 1), c:c + THIRD].rearrange("p o n -> p (o n)"))\
                    .then_inc(adj_landed[r % ADJ_RING], 16)

            def load_x(i, g):
                wait(sp, hT_ready, i, 2, g - 1)
                sp.dma_start(x_norm[:, g % 2], group_of(x_view, i, g)).then_inc(x_landed[g % 2], 16)

            def load_res(i, g):
                wait(sp, result_ready, i, 2, g - 1)
                sp.dma_start(x_res[:, g % 2], group_of(x_view, i, g)).then_inc(res_landed[g % 2], 16)

            load_x(0, 0)

            def load_input(c):
                part = slice(c * BLOCKS // 4, (c + 1) * BLOCKS // 4)
                sp.dma_start(inp_sb[:, part, :], inp_view[:, part, :]).then_inc(inp_landed[c], 16)

            load_input(0)
            sp.dma_start(w_sb[:], weight).then_inc(w_landed, 16)

            def step(i, s):
                if isinstance(i, int) and i == 0 and s in (4, 8):
                    load_input(s // 4)
                if isinstance(i, int) and i == 0 and s == 8:
                    load_input(3)
                if s % 4 == 0 and live(i, s // 4, BODY_THIRDS, STEPS // 4):
                    load_adj(i, s // 4)
                g = s // GROUP_STEPS
                if s % GROUP_STEPS == 4 and live(i, g + 1, 2, GROUPS):
                    load_x(i, g + 1)
                if s % GROUP_STEPS == 10 and live(i, g - 1, 2, GROUPS):
                    load_res(i, g - 1)

            run(sp, step)
            for c in range(2):
                sp.wait_ge(stored[c], 16 * GROUPS // 2)

        @block.gpsimd
        def _(pool):
            pool.memset(minus_half[:], -0.5).then_inc(half_ready, 1)
            pool.memset(big[:], BIG).then_inc(big_ready, 1)
            pool.memset(ident[:], 0.0).then_inc(ident_blank, 1)
            pool.wait_ge(ident_blank, 1)
            pool.affine_select(out=ident[:], in_=ident[:], compare_op=ALU.not_equal, fill=1.0, base=0,
                               pattern=[[-1, P]], channel_multiplier=1).then_inc(ident_ready, 1)
            pool.wait_ge(half_ready, 1)

            def invert_deviation(i, g):
                wait(pool, moments_ready, i, 2, g + 1)
                wait(pool, norm_ready, i, 2, g)
                detach(pool)
                pool.tensor_scalar(var_eps[:], moments[:, :, 1], EPS, None, ALU.add).then_inc(var_ready, 1)
                wait(pool, var_ready, i, 2, g + 1)
                pool.tensor_tensor(rstd[:], var_eps[:], minus_half[:], ALU.pow).then_inc(rstd_ready, 1)

            invert_deviation(0, 0)

            def normalise(i, g):
                wait(pool, rstd_ready, i, 2, g + 1)
                detach(pool)
                for t in range(TILES):
                    v = x_norm[:, g % 2, t, :]
                    mm = pool.tensor_scalar(v, v, moments[:, t, 0:1], rstd[:, t:t + 1], ALU.subtract, ALU.mult)
                mm.then_inc(norm_ready, 1)

            def odd_penalty(i, r):
                e = 2 * r + 1
                wait(pool, adj_landed[r % ADJ_RING], i, 16 * BODY_THIRDS // ADJ_RING, 16 * (r // ADJ_RING + 1))
                wait(pool, masked, i, BODY // 2, e - PENALTY_RING + 1)
                detach(pool)
                pool.tensor_scalar(penalty[:, e % PENALTY_RING, :], adj_sb[:, r % ADJ_RING, PAIR:THIRD], 0.0, BIG,
                                   ALU.is_le, ALU.mult).then_inc(odd_penalty_ready, 1)

            def give_mean(i, g):
                wait(pool, sum_ready, i, 2, g + 1)
                detach(pool)
                pool.tensor_scalar(no_edges[:], row_sum[:, g % 2, :], 1.0, None, ALU.is_le)\
                    .then_inc(no_edges_found, 1)
                wait(pool, no_edges_found, i, 2, g + 1)
                detach(pool)
                for t in range(TILES):
                    mm = pool.tensor_scalar(mean_part[:, t, :], val_mean[:], no_edges[:, t:t + 1], None, ALU.mult)
                mm.then_inc(mean_part_ready, 1)
                wait(pool, mean_part_ready, i, 2, g + 1)
                wait(pool, res_landed[g % 2], i, 16, 16 * (g // 2 + 1))
                pool.tensor_tensor(x_res[:, g % 2], x_res[:, g % 2], mean_part[:], ALU.add).then_inc(res_ready, 1)

            pool.memset(ones[:], 1.0).then_inc(ones_ready, 1)
            pool.memset(part_sum[:, :, PAIRS:], TINY).then_inc(tiny_ready, 1)

            def step(i, s):
                if s % 4 == 0 and live(i, s // 4, BODY_THIRDS, STEPS // 4):
                    odd_penalty(i, s // 4)
                g = s // GROUP_STEPS
                if s % GROUP_STEPS == 4 and live(i, g + 1, 2, GROUPS):
                    invert_deviation(i, g + 1)
                    normalise(i, g + 1)
                if s % GROUP_STEPS == 16 and live(i, g - 1, 2, GROUPS):
                    if isinstance(i, int) and i == 0 and g == 1:
                        pool.wait_ge(mean_ready, 1)
                    give_mean(i, g - 1)

            run(pool, step)

        @block.tensor
        def _(pe):
            def turn_keys(c):
                if c >= CHUNKS:
                    return
                if c % 3 == 0:
                    pe.wait_ge(inp_landed[c // 3], 16)
                if c >= 2:
                    pe.wait_ge(k_lo_ready, c - 1)
                for b in range(4):
                    mm = pe.transpose(ps_turn[:, c % 2, b * P:(b + 1) * P], inp_sb[:, 4 * c + b, :], ident[:])
                mm.then_inc(keys_turned, 1)

            def turn_h(i, g):
                wait(pe, norm_ready, i, 2, g + 1)
                wait(pe, result_ready, i, 2, g - 2)
                wait(pe, q_lo_ready, i, 2, g)
                for t in range(TILES):
                    mm = pe.transpose(ps_misc[:, t * P:(t + 1) * P], x_norm[:, g % 2, t, :], ident[:])
                mm.then_inc(hT_ready, 1)

            def project_q(i, g):
                wait(pe, hT_copied, i, 2, g + 1)
                pe.matmul(ps_misc[:, ROWS:2 * ROWS], w_sb[:], hT[:], start=True, stop=True).then_inc(qT_ready, 1)

            def sum_values(c):
                if not 0 <= c < CHUNKS:
                    return
                pe.wait_ge(ones_ready, 1)
                pe.wait_ge(v_lo_ready, c + 1)
                for b in range(4 * c, 4 * c + 4):
                    for v in range(2):
                        mm = pe.matmul(ps_acc[:, 0:D], ones[:], val[v][:, b, :],
                                       start=(b == 0 and v == 0), stop=(b == BLOCKS - 1 and v == 1))
                if c == CHUNKS - 1:
                    mm.then_inc(mean_summed, 1)

            def scores(i, k):
                slot, half = k // 2 % 2, k % 2
                if half == 0:
                    wait(pe, masked, i, BODY // 2, k // 2 - 1)
                if k % GROUP_STEPS == 0:
                    wait(pe, q_lo_ready, i, 2, k // GROUP_STEPS + 1)
                g, t, c = k // GROUP_STEPS % 2, k // CHUNKS % TILES, k % CHUNKS
                for n, (qp, kp) in enumerate(((0, 0), (0, 1), (1, 0))):
                    mm = pe.matmul(ps_scores[:, slot, half * CHUNK:(half + 1) * CHUNK],
                                   qT[qp][:, g, t * P:(t + 1) * P], kT[kp][:, c * CHUNK:(c + 1) * CHUNK],
                                   start=(n == 0), stop=(n == 2))
                if half == 1:
                    mm.then_inc(scores_ready, 1)

            def turn(i, k):
                g, j = k // GROUP_STEPS, k % GROUP_STEPS
                if j % 4 == 0:
                    wait(pe, probs_ready, i, BODY // 2, PAIRS * (TILES * g + 1) + j // 4 + 1)
                wait(pe, lo_ready, i, BODY, k - 1)
                for b in range(2):
                    for t in range(TILES):
                        at = (b * TILES + t) * P
                        col = (2 * j + b) * P
                        mm = pe.transpose(ps_turn[:, k % 2, at:at + P],
                                          probs[:, (TILES * g + t) % SLOTS, col:col + P], ident[:])
                mm.then_inc(turned, 1)

            def weigh(i, k):
                g, j = k // GROUP_STEPS, k % GROUP_STEPS
                wait(pe, lo_ready, i, BODY, k + 1)
                if j == 0:
                    wait(pe, acc_copied, i, 2, g)
                r = k % PART_RING
                for b in range(2):
                    for n, (v, p) in enumerate(((1, part_hi), (0, part_hi), (0, part_lo))):
                        mm = pe.matmul(ps_acc[:, 0:ROWS], val[v][:, 2 * j + b, :],
                                       p[:, r, b * ROWS:(b + 1) * ROWS],
                                       start=(j == 0 and b == 0 and n == 0),
                                       stop=(j == GROUP_STEPS - 1 and b == 1 and n == 2))
                mm.then_inc(weighed, 1)

            def turn_back(i, g):
                wait(pe, acc_copied, i, 2, g + 1)
                for t in range(TILES):
                    mm = pe.transpose(ps_misc[:, t * P:(t + 1) * P], accT_sb[:, t * P:(t + 1) * P], ident[:])
                mm.then_inc(acc_turned, 1)

            pe.wait_ge(ident_ready, 1)
            turn_keys(0)
            turn_h(0, 0)
            pe.wait_ge(w_landed, 16)
            project_q(0, 0)
            turn_keys(1)

            def step(i, s):
                if isinstance(i, int) and i == 0:
                    if s < CHUNKS:
                        pe.wait_ge(k_lo_ready, s + 1)
                if live(i, s, BODY, STEPS):
                    scores(i, s)
                if isinstance(i, int) and i == 0:
                    turn_keys(s + 2)
                    sum_values(s - SUM_AT)
                k = s - LAG - WEIGH
                if (k - 1) % GROUP_STEPS == 0 and live(i, k - 1, BODY, STEPS):
                    if isinstance(i, int) and i == 0:
                        pe.wait_ge(mean_ready, 1)
                    weigh(i, k - 1)
                if live(i, s - LAG, BODY, STEPS):
                    turn(i, s - LAG)
                if k % GROUP_STEPS != 0 and live(i, k, BODY, STEPS):
                    weigh(i, k)
                g = s // GROUP_STEPS
                if s % GROUP_STEPS == END + 1 and live(i, g - 2, 2, GROUPS):
                    turn_back(i, g - 2)
                if s % GROUP_STEPS == 12 and live(i, g + 1, 2, GROUPS):
                    turn_h(i, g + 1)
                if s % GROUP_STEPS == 14 and live(i, g + 1, 2, GROUPS):
                    project_q(i, g + 1)

            run(pe, step)

        @block.scalar
        def _(act):
            def copy_h(i, g):
                wait(act, hT_ready, i, 2, g + 1)
                act.activation(hT[:], ps_misc[:, 0:ROWS], ACT.Relu).then_inc(hT_copied, 1)

            def take_q_hi(i, g):
                wait(act, qT_ready, i, 2, g + 1)
                wait(act, scores_ready, i, BODY // 2, (g - 1) * GROUP_STEPS // 2)
                act.activation(qT[0][:, g % 2, :], ps_misc[:, ROWS:2 * ROWS], ACT.Copy).then_inc(q_hi_ready, 1)

            def even_penalty(i, r):
                e = 2 * r
                wait(act, adj_landed[r % ADJ_RING], i, 16 * BODY_THIRDS // ADJ_RING, 16 * (r // ADJ_RING + 1))
                wait(act, masked, i, BODY // 2, e - PENALTY_RING + 1)
                act.activation(penalty[:, e % PENALTY_RING, :], adj_sb[:, r % ADJ_RING, 0:PAIR], ACT.Relu,
                               scale=-BIG, bias=big[:]).then_inc(even_penalty_ready, 1)

            def exponentiate(i, e):
                t, b = e // PAIRS, e % PAIRS
                if b == 0:
                    wait(act, max_found, i, SLOTS, t + 1)
                    act.activation(exp_bias[:, t % SLOTS:t % SLOTS + 1], row_max[:, t % SLOTS:t % SLOTS + 1],
                                   ACT.Copy, bias=LIFT, scale=-1.0 / TEMPERATURE).then_inc(exp_bias_ready, 1)
                    wait(act, exp_bias_ready, i, SLOTS, t + 1)
                    wait(act, sum_ready, i, 2, t // TILES - 1)
                v = probs[:, t % SLOTS, b * PAIR:(b + 1) * PAIR]
                act.activation(v, v, ACT.Exp, bias=exp_bias[:, t % SLOTS:t % SLOTS + 1], scale=1.0 / TEMPERATURE,
                               accum_out=part_sum[:, t % SLOTS, b:b + 1]).then_inc(probs_ready, 1)

            def take_hi(i, k):
                wait(act, turned, i, BODY, k + 1)
                wait(act, weighed, i, BODY, k - PART_RING + 1)
                act.activation(part_hi[:, k % PART_RING, :], ps_turn[:, k % 2, :], ACT.Copy).then_inc(hi_ready, 1)

            def copy_acc(i, g):
                wait(act, weighed, i, BODY, (g + 1) * GROUP_STEPS)
                wait(act, acc_turned, i, 2, g)
                act.activation(accT_sb[:], ps_acc[:, 0:ROWS], ACT.Copy).then_inc(acc_copied, 1)

            def store(i, g):
                wait(act, result_ready, i, 2, g + 1)
                act.dma_start(group_of(out_view, i, g), result[:, g % 2]).then_inc(stored[g % 2], 16)

            def take_keys_hi(c):
                act.wait_ge(keys_turned, c + 1)
                act.activation(kT[0][:, c * CHUNK:(c + 1) * CHUNK], ps_turn[:, c % 2, :], ACT.Copy)\
                    .then_inc(k_hi_ready, 1)

            def take_values_hi(c):
                b = slice(4 * c, 4 * c + 4)
                act.activation(val[0][:, b, :], inp_sb[:, b, :], ACT.Copy).then_inc(v_hi_ready, 1)

            take_keys_hi(0)
            copy_h(0, 0)
            take_q_hi(0, 0)
            take_keys_hi(1)
            act.wait_ge(big_ready, 1)

            def step(i, s):
                if isinstance(i, int) and i == 0:
                    if s == 0:
                        even_penalty(0, 0)
                    if 2 <= s < CHUNKS:
                        take_keys_hi(s)
                    if CHUNKS <= s < 2 * CHUNKS:
                        take_values_hi(s - CHUNKS)
                g = s // GROUP_STEPS
                if s % GROUP_STEPS == END and live(i, g - 2, 2, GROUPS):
                    copy_acc(i, g - 2)
                if live(i, s - LAG, BODY, STEPS):
                    take_hi(i, s - LAG)
                if s % 4 == 2 and live(i, s // 4 + 1, BODY_THIRDS, STEPS // 4):
                    even_penalty(i, s // 4 + 1)
                if isinstance(i, int) and i == 0 and s == SUM_AT + CHUNKS + 1:
                    act.wait_ge(mean_summed, 1)
                    act.activation(val_mean[:], ps_acc[:, 0:D], ACT.Copy, scale=1.0 / N).then_inc(mean_ready, 1)
                if s % 2 == 1 and live(i, (s - EXP_AT) // 2, BODY // 2, STEPS // 2):
                    exponentiate(i, (s - EXP_AT) // 2)
                if s % GROUP_STEPS == END + 4 and live(i, g - 2, 2, GROUPS):
                    store(i, g - 2)
                if s % GROUP_STEPS == 13 and live(i, g + 1, 2, GROUPS):
                    copy_h(i, g + 1)
                if s % GROUP_STEPS == 15 and live(i, g + 1, 2, GROUPS):
                    take_q_hi(i, g + 1)

            run(act, step)

        @block.vector
        def _(dve):
            def find_moments(i, g):
                wait(dve, x_landed[g % 2], i, 16, 16 * (g // 2 + 1))
                wait(dve, norm_ready, i, 2, g)
                for t in range(TILES):
                    dve.bn_stats(stats[:, t, :], x_norm[:, g % 2, t, :]).then_inc(stats_ready, 1)
                wait(dve, stats_ready, i, 2 * TILES, TILES * (g + 1))
                detach(dve)
                for t in range(TILES):
                    mm = dve.bn_aggr(moments[:, t, :], stats[:, t, :])
                mm.then_inc(moments_ready, 1)

            def take_q_lo(i, g):
                wait(dve, q_hi_ready, i, 2, g + 1)
                dve.tensor_tensor(qT[1][:, g % 2, :], ps_misc[:, ROWS:2 * ROWS], qT[0][:, g % 2, :],
                                  ALU.subtract).then_inc(q_lo_ready, 1)

            def mask(i, e):
                t, b = e // PAIRS, e % PAIRS
                wait(dve, scores_ready, i, BODY // 2, e + 1)
                wait(dve, (even_penalty_ready, odd_penalty_ready)[e % 2], i, BODY_THIRDS, e // 2 + 1)
                wait(dve, turned, i, BODY, (t - SLOTS) // TILES * GROUP_STEPS + 4 * b + 4)
                detach(dve)
                dve.tensor_tensor_reduce(
                    probs[:, t % SLOTS, b * PAIR:(b + 1) * PAIR], ps_scores[:, e % 2, :],
                    penalty[:, e % PENALTY_RING, :], 1.0, NO_EDGE, ALU.subtract, ALU.max,
                    part_max[:, t % 2, b:b + 1]).then_inc(masked, 1)
                if b == PAIRS - 1:
                    wait(dve, masked, i, BODY // 2, e + 1)
                    dve.tensor_reduce(row_max[:, t % SLOTS:t % SLOTS + 1], part_max[:, t % 2, :], AX.X, ALU.max)\
                        .then_inc(max_found, 1)

            def take_lo(i, k):
                wait(dve, hi_ready, i, BODY, k + 1)
                dve.tensor_tensor(part_lo[:, k % PART_RING, :], ps_turn[:, k % 2, :], part_hi[:, k % PART_RING, :],
                                  ALU.subtract).then_inc(lo_ready, 1)

            def sum_rows(i, g):
                wait(dve, probs_ready, i, BODY // 2, (g + 1) * TILES * PAIRS)
                wait(dve, res_ready, i, 2, g - 1)
                wait(dve, result_ready, i, 2, g - 1)
                if isinstance(i, int):
                    dve.wait_ge(tiny_ready, 1)
                a = g * TILES % SLOTS
                dve.tensor_reduce(row_sum[:, g % 2, :], part_sum[:, a:a + TILES, :], AX.X, ALU.add).then_inc(sum_ready, 1)
                wait(dve, sum_ready, i, 2, g + 1)
                dve.reciprocal(inv_sum[:, g % 2, :], row_sum[:, g % 2, :]).then_inc(inv_ready, 1)

            def finish(i, g):
                wait(dve, inv_ready, i, 2, g + 1)
                wait(dve, acc_turned, i, 2, g + 1)
                wait(dve, res_ready, i, 2, g + 1)
                wait(dve, stored[g % 2], i, 16, 16 * (g // 2))
                for t in range(TILES):
                    mm = dve.scalar_tensor_tensor(out=result[:, g % 2, t, :], in0=ps_misc[:, t * P:(t + 1) * P],
                                                  scalar=inv_sum[:, g % 2, t:t + 1], in1=x_res[:, g % 2, t, :],
                                                  op0=ALU.mult, op1=ALU.add)
                mm.then_inc(result_ready, 1)

            def take_keys_lo(c):
                dve.wait_ge(k_hi_ready, c + 1)
                at = slice(c * CHUNK, (c + 1) * CHUNK)
                dve.tensor_tensor(kT[1][:, at], ps_turn[:, c % 2, :], kT[0][:, at], ALU.subtract)\
                    .then_inc(k_lo_ready, 1)

            def take_values_lo(c):
                dve.wait_ge(v_hi_ready, c + 1)
                b = slice(4 * c, 4 * c + 4)
                dve.tensor_tensor(val[1][:, b, :], inp_sb[:, b, :], val[0][:, b, :], ALU.subtract)\
                    .then_inc(v_lo_ready, 1)

            find_moments(0, 0)
            dve.wait_ge(rstd_ready, 1)
            for t in range(TILES):
                v = x_norm[:, 0, t, :]
                mm = dve.tensor_scalar(v, v, moments[:, t, 0:1], rstd[:, t:t + 1], ALU.subtract, ALU.mult)
            mm.then_inc(norm_ready, 1)
            take_keys_lo(0)
            take_q_lo(0, 0)
            take_keys_lo(1)

            def step(i, s):
                if isinstance(i, int) and i == 0:
                    if 2 <= s < CHUNKS:
                        take_keys_lo(s)
                    if CHUNKS <= s < 2 * CHUNKS:
                        take_values_lo(s - CHUNKS)
                    if s == 2 * CHUNKS:
                        dve.wait_ge(v_lo_ready, CHUNKS)
                g = s // GROUP_STEPS
                if s % 2 == 0 and live(i, s // 2 - 1, BODY // 2, STEPS // 2):
                    mask(i, s // 2 - 1)
                if live(i, s - LAG, BODY, STEPS):
                    take_lo(i, s - LAG)
                if s % GROUP_STEPS == 1 and live(i, g + 1, 2, GROUPS):
                    find_moments(i, g + 1)
                if s % GROUP_STEPS == 15 and live(i, g - 1, 2, GROUPS):
                    sum_rows(i, g - 1)
                if s % GROUP_STEPS == END + 2 and live(i, g - 2, 2, GROUPS):
                    finish(i, g - 2)
                if s % GROUP_STEPS == 16 and live(i, g + 1, 2, GROUPS):
                    take_q_lo(i, g + 1)

            run(dve, step)


_INS = ["x", "adj", "L0_gnn_input", "L0_gnn_weight"]


def kernel(**inputs):
    import numpy as _np
    import concourse.bacc as _bacc
    from concourse import mybir as _mybir
    from concourse.bass_utils import run_bass_kernel_spmd as _run

    nc = _bacc.Bacc("TRN2", target_bir_lowering=False, num_devices=1)
    arrays, args = {}, []
    for name in _INS:
        a = _np.ascontiguousarray(inputs[name])
        arrays[f"in_{name}_dram"] = a
        args.append(nc.dram_tensor(f"in_{name}_dram", a.shape, _mybir.dt.from_np(a.dtype), kind="ExternalInput").ap())
    out = nc.dram_tensor("out_dram", inputs["x"].shape, _mybir.dt.float32, kind="ExternalOutput").ap()
    adjacency_attention(nc, *args, out)
    r = _run(nc, [arrays], core_ids=[0])
    return r.results[0]["out_dram"]
```
